# Optimizing a Trainium2 kernel written in Bass

```python
import numpy as np
import jax
import jax.numpy as jnp

def _softmax(x, axis=-1):
    return jax.nn.softmax(x, axis=axis)

def _gelu(x):
    return jax.nn.gelu(x, approximate=True)

def _silu(x):
    return jax.nn.silu(x)

def _sigmoid(x):
    return jax.nn.sigmoid(x)

def _layernorm(x, axis=-1, eps=1e-05):
    m = jnp.mean(x, axis=axis, keepdims=True)
    v = jnp.var(x, axis=axis, keepdims=True)
    return (x - m) / jnp.sqrt(v + eps)

def _scatter_add(tgt, idx, src, axis=0):
    return tgt.at[idx].add(src)

def _segment_sum(src, seg, n):
    return jax.ops.segment_sum(src, seg, n)
kernel_name = 'mk_rec_standalone_d1_rec_r8_0b0195'

def setup_inputs(seed: int=0):
    np.random.seed(seed)
    _w = jnp.asarray

    def _rec_inputs():
        import jax
        import jax.numpy as jnp
        _rk = jax.random.key(seed)
        r_inputs = -0.000849101 + 1.0004 * jax.random.normal(jax.random.fold_in(_rk, 1), (512, 39, 16), jnp.float32)
        return r_inputs
    r_inputs = _rec_inputs()

    def _L0_rec_setup():
        import jax, jax.numpy as jnp
        import numpy as np
        B, F0, D = (256, 39, 16)
        CROSS = [128, 128, 128]
        key = jax.random.key(seed)
        k0, k1, k2, k3 = jax.random.split(key, 4)
        inputs = jax.random.normal(k0, (B, F0, D), dtype=jnp.float32)
        f0 = jax.random.normal(k1, (F0 * F0, CROSS[0]), dtype=jnp.float32) * 0.05
        f1 = jax.random.normal(k2, (CROSS[0] * F0, CROSS[1]), dtype=jnp.float32) * 0.05
        f2 = jax.random.normal(k3, (CROSS[1] * F0, CROSS[2]), dtype=jnp.float32) * 0.05
        return {'inputs': inputs, 'f0': f0, 'f1': f1, 'f2': f2}
    _L0_rec_all = _L0_rec_setup()
    _L0_rec_in = {k: v for k, v in _L0_rec_all.items() if k in ('f0', 'f1', 'f2')}
    del _L0_rec_all
    return {'r_inputs': r_inputs, 'L0_rec_f0': _L0_rec_in['f0'], 'L0_rec_f1': _L0_rec_in['f1'], 'L0_rec_f2': _L0_rec_in['f2']}

def reference(r_inputs, L0_rec_f0, L0_rec_f1, L0_rec_f2):
    import jax
    import jax.numpy as jnp

    def _L0_rec_ref(inputs, f0, f1, f2):
        import jax, jax.numpy as jnp
        import numpy as np
        B, F0, D = (256, 39, 16)
        CROSS = [128, 128, 128]
        filters = [f0, f1, f2]
        x0 = inputs
        xk = inputs
        outs = []
        for W in filters:
            b, f, d = x0.shape
            g = xk.shape[1]
            z = jnp.einsum('bfd,bgd->bfgd', x0, xk).reshape(b, f * g, d)
            cur = jnp.einsum('bpd,pm->bmd', z, W)
            outs.append(cur)
            xk = cur
        result = jnp.concatenate(outs, axis=1)
        return jnp.sum(result, axis=-1)
    y = _L0_rec_ref(r_inputs, L0_rec_f0, L0_rec_f1, L0_rec_f2)
    return y

_drawn_inputs = setup_inputs


def setup_inputs(seed=0):
    import zlib

    import numpy as np

    out = dict(_drawn_inputs(seed))
    spreads = {}
    factors = {}
    for name, (base, spread) in spreads.items():
        noise = np.random.default_rng([zlib.crc32(name.encode()), seed]).standard_normal(out[name].shape)
        drawn = base * np.exp(spread * noise) if base else spread * noise
        out[name] = jnp.asarray(drawn.astype(out[name].dtype))
    for name, factor in factors.items():
        out[name] = (out[name] * factor).astype(out[name].dtype)
    return out
```

```python
from contextlib import ExitStack

import concourse.bass as bass
from concourse import mybir

ALU = mybir.AluOpType
ACT = mybir.ActivationFunctionType
F32 = mybir.dt.float32
F32R = mybir.dt.float32r
AX_X = mybir.AxisListType.X

B, F, D, M = 512, 39, 16, 128
N = B * D
P = 128
CHUNK = 512
CHUNKS = N // CHUNK
TILE = 128
TPC = CHUNK // TILE
BT = TILE // D
BC = CHUNK // D
SHIFTS = F // 2 + 1
SPT = P // F
ROWS = SPT * F
PT = -(-SHIFTS // SPT)
F1 = F + 1
GF = 4
VG = [(f, GF) for f in range(0, 20, GF)]
SG = [(f, min(GF, F - f)) for f in range(20, F, GF)]
NG = len(VG)
GPC = NG * TPC
RING = 3
ZR = 3
Z_SLOT = [0, 1, 2, 0, 1, 2, 1]
BANK_OF = [0, 1, 2, 0, 1, 2, 1, 0, 2, 1]

Z_AFTER = {(0, 0): 0, (0, 2): 1, (0, 4): 2, (1, 2): 3, (1, 4): 4, (2, 0): 5, (2, 2): 6}
L1_AFTER = {(0, 2): 0, (0, 4): 1, (1, 1): 2, (1, 4): 3, (2, 1): 4, (2, 2): 5, (2, 4): 6}
SPLIT_TILE = 3


def rows_of(t):
    return F * min(SPT, SHIFTS - SPT * t)


def uses_back(places, i):
    return next(k for k in range(1, len(places) + 1) if places[(i - k) % len(places)] == places[i])


def cin(nc, xrows, xcols, xdiag, w0, w1, w2, yt):
    with ExitStack() as ctx:
        def sb(name, shape, dt=F32):
            return ctx.enter_context(nc.sbuf_tensor(name, shape, dt))

        def ps(name):
            return ctx.enter_context(nc.psum_tensor(name, [P, 512], F32))

        def sem(name):
            return ctx.enter_context(nc.semaphore(name))

        w1h = sb("w1h", [P, F * M], F32R)
        w1l = sb("w1l", [P, F * M], F32R)
        w2s = sb("w2s", [P, F * M])
        S = sb("S", [P, F1, B])
        early = S[:, :, :].rearrange("p f b -> p (f b)")
        w1raw = early[:, 0:F * M]
        w0pair = [early[0:ROWS, F * M + i * PT * M:F * M + (i + 1) * PT * M] for i in range(2)]
        w0sym = sb("w0sym", [ROWS, PT * M])
        xshift = [sb(f"xshift{t}", [ROWS, CHUNK]) for t in range(PT)]
        xbase = [sb(f"xbase{i}", [ROWS, CHUNK]) for i in range(2)]
        z = [sb(f"z{i}", [ROWS, CHUNK]) for i in range(ZR)]
        x1h = [sb(f"x1h{i}", [P, CHUNK], F32R) for i in range(2)]
        x1l = [sb(f"x1l{i}", [P, CHUNK], F32R) for i in range(2)]
        xcol = [sb(f"xcol{i}", [P, TPC * F]) for i in range(2)]
        xd = [sb(f"xd{i}", [P, BT * F1]) for i in range(2)]
        acc = [sb(f"acc{i}", [P, GF * M]) for i in range(2)]
        acc_half = sb("acc_half", [P, GF * M // 2])
        acc_sum = sb("acc_sum", [P, M])
        prod = [sb(f"prod{i}", [P, len(SG), GF * M]) for i in range(2)]
        q = [sb(f"q{i}", [P, M]) for i in range(2)]
        x2 = [sb(f"x2{i}", [P, M]) for i in range(2)]
        y1 = sb("y1", [P, B])
        y3 = prod[0][:, 0, :]

        vbank = [ps(f"vbank{i}") for i in range(RING)]
        sbank = [ps(f"sbank{i}") for i in range(RING)]
        l1bank = ps("l1bank")
        Sbank = ps("Sbank")

        w0_loaded = sem("w0_loaded")
        w1_loaded = [sem(f"w1_loaded{i}") for i in range(2 * NG)]
        w2_loaded = sem("w2_loaded")
        xshift_loaded = [sem(f"xshift_loaded{t}") for t in range(PT)]
        xbase_loaded = [sem(f"xbase_loaded{i}") for i in range(2)]
        xcol_loaded = [sem(f"xcol_loaded{i}") for i in range(2)]
        xd_loaded = [sem(f"xd_loaded{i}") for i in range(2)]
        w0_ready = sem("w0_ready")
        w1h_ready = sem("w1h_ready")
        w1l_ready = sem("w1l_ready")
        z_ready = sem("z_ready")
        l1_steps = sem("l1_steps")
        x1h_ready = sem("x1h_ready")
        x1l_ready = sem("x1l_ready")
        l1_free = sem("l1_free")
        v_full = sem("v_full")
        v_half = sem("v_half")
        v_done = sem("v_done")
        half_ready = sem("half_ready")
        sum_ready = sem("sum_ready")
        s_full = sem("s_full")
        s_done = sem("s_done")
        pool_step = sem("pool_step")
        q_ready = sem("q_ready")
        x2_ready = sem("x2_ready")
        S_full = sem("S_full")
        S_stored = sem("S_stored")
        y3_full = sem("y3_full")
        y3_ready = sem("y3_ready")
        y_stored = sem("y_stored")

        pieces = [g for pair in zip(VG, SG) for g in pair]

        def count(ck, per_chunk, more):
            return ck[0] * per_chunk + (ck[1] * per_chunk + more)

        block = ctx.enter_context(nc.Block())

        @block.sync
        def _(sp):
            def load_shift(t, ck):
                for j in range(rows_of(t) // F):
                    r = SPT * t + j
                    sp.dma_start(xshift[t][j * F:(j + 1) * F, :],
                                 xrows[r:r + F, bass.ds(count(ck, CHUNK, 0), CHUNK)]).then_inc(xshift_loaded[t], 16)

            def load_base(par, ck):
                for j in range(SPT):
                    sp.dma_start(xbase[par][j * F:(j + 1) * F, :],
                                 xrows[0:F, bass.ds(count(ck, CHUNK, 0), CHUNK)]).then_inc(xbase_loaded[par], 16)

            def load_cols(par, ck):
                sp.dma_start(xcol[par][:, :], xcols[:, bass.ds(count(ck, TPC * F, 0), TPC * F)]) \
                  .then_inc(xcol_loaded[par], 16)

            def load_diag(par, tile):
                sp.dma_start(xd[par][:, :], xdiag[:, bass.ds(tile, BT * F1)]).then_inc(xd_loaded[par], 16)

            sp.dma_start(w0pair[0], w0[0, :, :]).then_inc(w0_loaded, 16)
            load_base(0, (0, 0))
            for t in range(PT):
                load_shift(t, (0, 0))
                if t == 0:
                    sp.dma_start(w0pair[1], w0[1, :, :]).then_inc(w0_loaded, 16)
            load_cols(0, (0, 0))
            for i, (f, n) in enumerate(pieces):
                sp.dma_start(w1raw[:, f * M:(f + n) * M], w1[:, f * M:(f + n) * M]).then_inc(w1_loaded[i], 16)
            load_base(1, (1, 0))
            for t in range(PT):
                sp.wait_ge(z_ready, t + 1)
                load_shift(t, (1, 0))
            load_cols(1, (1, 0))
            load_diag(0, 0)
            load_diag(1, BT * F1)
            sp.dma_start(w2s[:, :], w2[:, :]).then_inc(w2_loaded, 16)

            def chunk(ck, par, first=False, last=False, tail=False):
                if not first and not last:
                    sp.wait_ge(v_done, count(ck, GPC, 0))
                    sp.wait_ge(s_done, count(ck, GPC, 0))
                    load_cols(1 - par, (ck[0], ck[1] + 1))
                for j in range(TPC):
                    if not last and not tail:
                        if j == 0:
                            load_base(par, (ck[0], ck[1] + 2))
                        for (jj, g), t in Z_AFTER.items():
                            if jj == j:
                                sp.wait_ge(z_ready, count(ck, PT, PT + t + 1))
                                load_shift(t, (ck[0], ck[1] + 2))
                    if not (first and j == 0) and not (last and j == TPC - 1):
                        sp.wait_ge(S_full, count(ck, TPC, j))
                        load_diag((j + 1) % 2, count(ck, TPC * BT * F1, (j + 1) * BT * F1))

            chunk((0, 0), 0, first=True)
            with sp.Fori(1, CHUNKS - 4, 2) as c:
                chunk((c, 0), 1)
                chunk((c, 1), 0)
            chunk((CHUNKS - 3, 0), 1)
            chunk((CHUNKS - 2, 0), 0, tail=True)
            chunk((CHUNKS - 1, 0), 1, last=True)
            sp.wait_ge(l1_free, CHUNKS)
            sp.dma_start(yt[0:M, :], y1[:, :]).then_inc(y_stored, 16)
            sp.wait_ge(S_stored, CHUNKS * TPC)
            sp.dma_start(yt[M:2 * M, :], S[:, F, :]).then_inc(y_stored, 16)
            sp.wait_ge(y3_ready, 1)
            sp.dma_start(yt[2 * M:3 * M, :], y3).then_inc(y_stored, 16)
            sp.wait_ge(y_stored, 3 * 16)

        @block.tensor
        def _(pe):
            def layer1(t, ck):
                r = rows_of(t)
                pe.wait_ge(z_ready, count(ck, PT, t + 1))
                mm = pe.matmul(l1bank[:, :], w0sym[0:r, t * M:(t + 1) * M], z[Z_SLOT[t]][0:r, :],
                               start=(t == 0), stop=(t == PT - 1))
                mm.then_inc(l1_steps, 1)

            def scores(ck, par, j, g, kind, bank, full, done, f, n, first):
                g2 = NG * (j % 2) + g
                back = uses_back(BANK_OF, g2)
                if not (first and NG * j + g < back):
                    pe.wait_ge(done, count(ck, GPC, NG * j + g - back + 1))
                out = bank[BANK_OF[g2]][:, 0:n * M]
                cols = slice(j * TILE, (j + 1) * TILE)
                wc = slice(f * M, (f + n) * M)
                if first and j == 0:
                    pe.wait_ge(w1h_ready, 2 * g + kind + 1)
                pe.matmul(out, x1h[par][:, cols], w1h[:, wc], start=True, stop=False)
                pe.matmul(out, x1l[par][:, cols], w1h[:, wc], start=False, stop=False)
                if first and j == 0:
                    pe.wait_ge(w1l_ready, 2 * g + kind + 1)
                pe.matmul(out, x1h[par][:, cols], w1l[:, wc], start=False, stop=True).then_inc(full, 1)

            def sum_d(ck, j, only=False):
                par = j % 2
                pe.wait_ge(x2_ready, count(ck, TPC, j + 1))
                pe.wait_ge(xd_loaded[par], count(ck, 16 * TPC // 2, 16 * (j // 2 + 1)))
                if not only:
                    pe.wait_ge(S_stored, count(ck, TPC, j))
                pe.matmul(Sbank[:, 0:BT * F1], x2[par][:, :], xd[par][:, :], start=True, stop=True).then_inc(S_full, 1)

            def chunk(ck, par, first=False, last=False):
                pe.wait_ge(x1h_ready, count(ck, 1, 1))
                pe.wait_ge(x1l_ready, count(ck, 1, 1))
                for j in range(TPC):
                    for g in range(NG):
                        scores(ck, par, j, g, 0, vbank, v_full, v_done, *VG[g], first)
                        scores(ck, par, j, g, 1, sbank, s_full, s_done, *SG[g], first)
                        if g == NG - 1 and not (first and j == 0):
                            sum_d(ck, j - 1, only=first and j == 1)
                        if not last and (j, g) in L1_AFTER:
                            t = L1_AFTER[j, g]
                            if t == 0:
                                pe.wait_ge(l1_free, count(ck, 1, 1))
                            layer1(t, (ck[0], ck[1] + 1))

            pe.wait_ge(w0_ready, 1)
            for t in range(PT):
                layer1(t, (0, 0))
            chunk((0, 0), 0, first=True)
            with pe.Fori(1, CHUNKS - 2, 2) as c:
                chunk((c, 0), 1)
                chunk((c, 1), 0)
            chunk((CHUNKS - 1, 0), 1, last=True)
            sum_d((CHUNKS - 1, 0), TPC - 1)
            pe.wait_ge(w2_loaded, 16)
            pe.wait_ge(S_stored, CHUNKS * TPC)
            for f in range(F):
                mm = pe.matmul(l1bank[:, :], w2s[:, f * M:(f + 1) * M], S[:, f, :], start=(f == 0), stop=(f == F - 1))
            mm.then_inc(y3_full, 1)

        @block.scalar
        def _(act):
            def split_x1(ck, par):
                act.wait_ge(l1_steps, count(ck, PT, PT))
                act.activation(x1h[par][:, :], l1bank[:, :], ACT.Copy).then_inc(x1h_ready, 1)

            def store_S(ck, j):
                act.wait_ge(S_full, count(ck, TPC, j + 1))
                act.activation(S[:, :, bass.ds(count(ck, BC, j * BT), BT)],
                               Sbank[:, 0:BT * F1].rearrange("p (b f) -> p f b", f=F1), ACT.Copy).then_inc(S_stored, 1)

            def chunk(ck, par, first=False, last=False):
                act.wait_ge(xcol_loaded[par], count(ck, 8, 8 if par else 16))
                for j in range(TPC):
                    if not (first and j < 2):
                        act.wait_ge(q_ready, count(ck, TPC, j - 1))
                    for g, (f0, n) in enumerate(SG):
                        act.wait_ge(s_full, count(ck, GPC, NG * j + g + 1))
                        for i in range(n):
                            op = act.activation(prod[j % 2][:, g, i * M:(i + 1) * M],
                                                sbank[BANK_OF[NG * (j % 2) + g]][:, i * M:(i + 1) * M], ACT.Copy,
                                                scale=xcol[par][:, j * F + f0 + i:j * F + f0 + i + 1])
                        op.then_inc(s_done, 1)
                        if g == 1 and not (first and j < 2):
                            store_S(ck, j - 2)
                        if not last and (j, g) == (SPLIT_TILE, 2):
                            split_x1((ck[0], ck[1] + 1), 1 - par)

            for i, (f, n) in enumerate(pieces):
                act.wait_ge(w1_loaded[i], 16)
                act.activation(w1h[:, f * M:(f + n) * M], w1raw[:, f * M:(f + n) * M], ACT.Copy).then_inc(w1h_ready, 1)
            split_x1((0, 0), 0)
            chunk((0, 0), 0, first=True)
            with act.Fori(1, CHUNKS - 2, 2) as c:
                chunk((c, 0), 1)
                chunk((c, 1), 0)
            chunk((CHUNKS - 1, 0), 1, last=True)
            for j in range(TPC - 2, TPC):
                store_S((CHUNKS - 1, 0), j)
            act.wait_ge(y3_full, 1)
            act.activation(y3, l1bank[:, :], ACT.Copy).then_inc(y3_ready, 1)

        @block.vector
        def _(dve):
            def products(t, ck, par, first=False):
                r = rows_of(t)
                if t == 0:
                    dve.wait_ge(xbase_loaded[par], count(ck, 8 * SPT, (8 if par else 16) * SPT))
                dve.wait_ge(xshift_loaded[t], count(ck, 16 * (r // F), 16 * (r // F)))
                back = uses_back(Z_SLOT, t)
                if not (first and t < back):
                    dve.wait_ge(l1_steps, count(ck, PT, t - back + 1))
                dve.tensor_tensor(z[Z_SLOT[t]][0:r, :], xbase[par][0:r, :], xshift[t][0:r, :], ALU.mult).then_inc(z_ready, 1)

            def split_x1(ck, par):
                dve.wait_ge(x1h_ready, count(ck, 1, 1))
                dve.tensor_tensor(x1l[par][:, :], l1bank[:, :], x1h[par][:, :].bitcast(F32), ALU.subtract) \
                   .then_inc(x1l_ready, 1)
                dve.tensor_reduce(y1[:, bass.ds(count(ck, BC, 0), BC)],
                                  l1bank[:, :].rearrange("p (b d) -> p b d", d=D), AX_X, ALU.add).then_inc(l1_free, 1)

            def fold(ck, j):
                H = GF * M // 2
                a = acc[j % 2]
                dve.wait_ge(v_done, count(ck, GPC, NG * (j + 1)))
                dve.tensor_tensor(acc_half[:, :], a[:, 0:H], a[:, H:2 * H], ALU.add).then_inc(half_ready, 1)

            def fold_again(ck, j):
                dve.wait_ge(half_ready, count(ck, TPC, j + 1))
                dve.tensor_tensor(acc_sum[:, :], acc_half[:, 0:M], acc_half[:, M:2 * M], ALU.add).then_inc(sum_ready, 1)

            def finish_x2(ck, j, early=False):
                i = j % 2
                dve.wait_ge(sum_ready, count(ck, TPC, j + 1))
                dve.wait_ge(q_ready, count(ck, TPC, j + 1))
                if not early:
                    dve.wait_ge(S_full, count(ck, TPC, j - 1))
                dve.tensor_tensor(x2[i][:, :], acc_sum[:, :], q[i][:, :], ALU.add).then_inc(x2_ready, 1)

            def scale_and_sum(ck, par, j, g):
                f0, n = VG[g]
                bank = vbank[BANK_OF[NG * (j % 2) + g]]
                dve.wait_ge(v_full, count(ck, GPC, NG * j + g + 1))
                for i in range(n):
                    a = acc[j % 2][:, i * M:(i + 1) * M]
                    x = xcol[par][:, j * F + f0 + i:j * F + f0 + i + 1]
                    src = bank[:, i * M:(i + 1) * M]
                    if g == 0:
                        op = dve.tensor_scalar(a, src, x, None, ALU.mult)
                    else:
                        if i == 0:
                            dve.wait_ge(v_half, count(ck, GPC, NG * j + g))
                        if i == n // 2:
                            dve.wait_ge(v_done, count(ck, GPC, NG * j + g))
                        op = dve.scalar_tensor_tensor(a, src, x, a, ALU.mult, ALU.add)
                    if i == n // 2 - 1:
                        op.then_inc(v_half, 1)
                op.then_inc(v_done, 1)

            def chunk(ck, par, first=False, last=False):
                dve.wait_ge(xcol_loaded[par], count(ck, 8, 8 if par else 16))
                for j in range(TPC):
                    for g in range(NG):
                        scale_and_sum(ck, par, j, g)
                        if not (first and j == 0):
                            if g == 0:
                                fold(ck, j - 1)
                            if g == 1:
                                fold_again(ck, j - 1)
                            if g == 2:
                                finish_x2(ck, j - 1, early=first and j < 3)
                        if not last and (j, g) in Z_AFTER:
                            products(Z_AFTER[j, g], (ck[0], ck[1] + 1), 1 - par)
                        if not last and (j, g) == (SPLIT_TILE, 2):
                            split_x1((ck[0], ck[1] + 1), 1 - par)

            dve.wait_ge(w0_loaded, 32)
            dve.tensor_tensor(w0sym[:, :], w0pair[0], w0pair[1], ALU.add).then_inc(w0_ready, 1)
            for t in range(PT):
                products(t, (0, 0), 0, first=True)
            for i, (f, n) in enumerate(pieces):
                if i == NG:
                    split_x1((0, 0), 0)
                wc = slice(f * M, (f + n) * M)
                dve.wait_ge(w1h_ready, i + 1)
                dve.tensor_tensor(w1l[:, wc], w1raw[:, wc], w1h[:, wc].bitcast(F32), ALU.subtract).then_inc(w1l_ready, 1)
            chunk((0, 0), 0, first=True)
            with dve.Fori(1, CHUNKS - 2, 2) as c:
                chunk((c, 0), 1)
                chunk((c, 1), 0)
            chunk((CHUNKS - 1, 0), 1, last=True)
            fold((CHUNKS - 1, 0), TPC - 1)
            fold_again((CHUNKS - 1, 0), TPC - 1)
            finish_x2((CHUNKS - 1, 0), TPC - 1)

        @block.gpsimd
        def _(pool):
            def sum_products(ck, j, early=False):
                p = prod[j % 2]
                H = GF * M // 2
                base = NG * j

                def add(out, a, b, after=None):
                    if after:
                        pool.wait_ge(pool_step, count(ck, TPC * 6, 6 * j + after))
                    return pool.tensor_tensor(out, a, b, ALU.add)

                pool.wait_ge(s_done, count(ck, GPC, base + 2))
                add(p[:, 0, :], p[:, 0, :], p[:, 1, :]).then_inc(pool_step, 1)
                pool.wait_ge(s_done, count(ck, GPC, base + 4))
                add(p[:, 2, :], p[:, 2, :], p[:, 3, :]).then_inc(pool_step, 1)
                add(p[:, 0, :], p[:, 0, :], p[:, 2, :], after=2).then_inc(pool_step, 1)
                add(p[:, 0, 0:H], p[:, 0, 0:H], p[:, 0, H:2 * H], after=3).then_inc(pool_step, 1)
                pool.wait_ge(s_done, count(ck, GPC, base + 5))
                add(p[:, 0, 0:H], p[:, 0, 0:H], p[:, 4, 0:H], after=4).then_inc(pool_step, 1)
                add(p[:, 0, 0:M], p[:, 0, 0:M], p[:, 0, M:2 * M], after=5).then_inc(pool_step, 1)
                if not early:
                    pool.wait_ge(x2_ready, count(ck, TPC, j - 1))
                add(q[j % 2][:, :], p[:, 0, 0:M], p[:, 4, H:H + M], after=6).then_inc(q_ready, 1)

            for j in range(TPC):
                sum_products((0, 0), j, early=j < 2)
            with pool.Fori(1, CHUNKS) as c:
                for j in range(TPC):
                    sum_products((c, 0), j)


_INS = ["xrows", "xcols", "xdiag", "w0", "w1", "w2"]


def kernel(r_inputs, L0_rec_f0, L0_rec_f1, L0_rec_f2):
    import numpy as np
    import concourse.bacc as bacc
    from concourse import mybir as mb
    from concourse.bass_utils import run_bass_kernel_spmd

    x = np.asarray(r_inputs)
    f0 = np.asarray(L0_rec_f0).reshape(F, F, M)
    rows = x.transpose(1, 0, 2).reshape(F, N)
    xrows = np.concatenate([rows, rows[:SHIFTS]], axis=0)
    tiles = x.transpose(0, 2, 1).reshape(N // TILE, TILE, F)
    xcols = tiles.transpose(1, 0, 2).reshape(TILE, -1)
    diag = np.zeros((TILE, N // TILE, BT, F1), x.dtype)
    for b in range(BT):
        diag[b * D:(b + 1) * D, :, b, :F] = tiles[:, b * D:(b + 1) * D, :].transpose(1, 0, 2)
        diag[b * D:(b + 1) * D, :, b, F] = 1
    w0 = np.zeros((2, PT * SPT, F, M), f0.dtype)
    fs = np.arange(F)
    for s in range(SHIFTS):
        w0[0, s] = f0[fs, (fs + s) % F]
        if s:
            w0[1, s] = f0[(fs + s) % F, fs]
    w0 = w0.reshape(2, PT, ROWS, M).transpose(0, 2, 1, 3).reshape(2, ROWS, PT * M)
    w1, w2 = (np.asarray(w).reshape(F, M, M).transpose(1, 0, 2).reshape(M, F * M) for w in (L0_rec_f1, L0_rec_f2))

    arrays = {n: np.ascontiguousarray(a) for n, a in zip(_INS, (xrows, xcols, diag.reshape(TILE, -1), w0, w1, w2))}
    nc = bacc.Bacc("TRN2", target_bir_lowering=False, num_devices=1)
    args = [nc.dram_tensor(n, a.shape, mb.dt.from_np(a.dtype), kind="ExternalInput").ap() for n, a in arrays.items()]
    yt = nc.dram_tensor("yt", (3 * M, B), mb.dt.float32, kind="ExternalOutput").ap()
    cin(nc, *args, yt)
    r = run_bass_kernel_spmd(nc, [arrays], core_ids=[0])
    return np.ascontiguousarray(r.results[0]["yt"].T)
```

```python
from contextlib import ExitStack

import concourse.bass as bass
from concourse import mybir

ALU = mybir.AluOpType
ACT = mybir.ActivationFunctionType
F32 = mybir.dt.float32
F32R = mybir.dt.float32r
AX_X = mybir.AxisListType.X

B, F, D, M = 512, 39, 16, 128
N = B * D
P = 128
CHUNK = 512
CHUNKS = N // CHUNK
TILE = 128
TPC = CHUNK // TILE
BT = TILE // D
BC = CHUNK // D
SHIFTS = F // 2 + 1
SPT = P // F
ROWS = SPT * F
PT = -(-SHIFTS // SPT)
F1 = F + 1
GF = 4
FV = 16
VG = [(f, GF) for f in range(0, FV, GF)]
SG = [(f, min(GF, F - f)) for f in range(FV, F, GF)]
NV, NS = len(VG), len(SG)
NG = NV + NS
IS_V = [0, 1, 0, 1, 0, 1, 0, 1, 0, 0]
GROUPS = []
for v in IS_V:
    GROUPS.append((v, sum(1 for k, _ in GROUPS if k == v)))
V_BANK = [0, 1, 2, 0, 1, 2, 0, 1]
S_BANK = [0, 1, 2, 0, 1, 2] * 2
RING = 3
ZR = 2

Z_AFTER = [0, 1, 2, 4, 5, 6, 8]
ZH_AFTER = [1, 3, 4, 7, 9, 10, 13]
ZL_AFTER = [1, 2, 4, 5, 6, 8, 9]
L1_AFTER = [3, 4, 6, 7, 9, 10, 12]
X1H_AFTER = (TPC - 1) * NS + 1
STEPS = 6
PROD_FREE = [None, 1, 3, 2, 5, 4]
X1L_AFTER = (TPC - 1) * NV + 1


def rows_of(t):
    return F * min(SPT, SHIFTS - SPT * t)


def uses_back(places, i):
    return next(k for k in range(1, len(places) + 1) if places[(i - k) % len(places)] == places[i])


def cin(nc, xrows, xcols, xdiag, w0, w1, w2, yt):
    with ExitStack() as ctx:
        def sb(name, shape, dt=F32):
            return ctx.enter_context(nc.sbuf_tensor(name, shape, dt))

        def ps(name):
            return ctx.enter_context(nc.psum_tensor(name, [P, 512], F32))

        def sem(name):
            return ctx.enter_context(nc.semaphore(name))

        w1h = sb("w1h", [P, F * M], F32R)
        w1l = sb("w1l", [P, F * M], F32R)
        w2s = sb("w2s", [P, F * M])
        S = sb("S", [P, F1, B])
        early = S[:, :, :].rearrange("p f b -> p (f b)")
        w1raw = early[:, 0:F * M]
        w0pair = [early[0:ROWS, F * M + i * PT * M:F * M + (i + 1) * PT * M] for i in range(2)]
        w0sym = early[0:ROWS, F * M + 2 * PT * M:F * M + 3 * PT * M]
        w0h = sb("w0h", [ROWS, PT * M], F32R)
        w0l = sb("w0l", [ROWS, PT * M], F32R)
        xshift = [sb(f"xshift{t}", [ROWS, CHUNK]) for t in range(PT)]
        xbase = [sb(f"xbase{i}", [ROWS, CHUNK]) for i in range(2)]
        zh = [sb(f"zh{i}", [ROWS, CHUNK], F32R) for i in range(ZR)]
        zl = [sb(f"zl{i}", [ROWS, CHUNK], F32R) for i in range(ZR)]
        x1h = [sb(f"x1h{i}", [P, CHUNK], F32R) for i in range(2)]
        x1l = [sb(f"x1l{i}", [P, CHUNK], F32R) for i in range(2)]
        xcol = [sb(f"xcol{i}", [P, TPC * F]) for i in range(2)]
        xd = [sb(f"xd{i}", [P, BT * F1]) for i in range(2)]
        acc = [sb(f"acc{i}", [P, GF * M]) for i in range(2)]
        acc_half = sb("acc_half", [P, GF * M // 2])
        acc_sum = sb("acc_sum", [P, M])
        prod0 = [sb(f"prod0{i}", [P, GF * M]) for i in range(2)]
        prod_rest = sb("prod_rest", [P, NS - 1, GF * M])
        q = [sb(f"q{i}", [P, M]) for i in range(2)]
        x2 = [sb(f"x2{i}", [P, M]) for i in range(2)]
        y1 = sb("y1", [P, B])
        y3 = prod0[0][:, :]

        vbank = [ps(f"vbank{i}") for i in range(RING)]
        sbank = [ps(f"sbank{i}") for i in range(RING)]
        l1bank = ps("l1bank")
        Sbank = ps("Sbank")

        w0_loaded = sem("w0_loaded")
        w1_loaded = [sem(f"w1_loaded{i}") for i in range(NG)]
        w2_loaded = sem("w2_loaded")
        xshift_loaded = [sem(f"xshift_loaded{t}") for t in range(PT)]
        xbase_loaded = [sem(f"xbase_loaded{i}") for i in range(2)]
        xcol_loaded = [sem(f"xcol_loaded{i}") for i in range(2)]
        xd_loaded = [sem(f"xd_loaded{i}") for i in range(2)]
        w0sym_ready = sem("w0sym_ready")
        w0h_ready = sem("w0h_ready")
        w0l_ready = sem("w0l_ready")
        w1h_ready = sem("w1h_ready")
        w1l_ready = sem("w1l_ready")
        z_ready = sem("z_ready")
        zh_ready = sem("zh_ready")
        zl_ready = sem("zl_ready")
        l1_steps = sem("l1_steps")
        x1h_ready = sem("x1h_ready")
        x1l_ready = sem("x1l_ready")
        l1_free = sem("l1_free")
        v_full = sem("v_full")
        v_half = sem("v_half")
        v_done = sem("v_done")
        half_ready = sem("half_ready")
        sum_ready = sem("sum_ready")
        s_full = sem("s_full")
        s_done = sem("s_done")
        pool_step = sem("pool_step")
        q_ready = sem("q_ready")
        x2_ready = sem("x2_ready")
        S_full = sem("S_full")
        S_stored = sem("S_stored")
        y3_full = sem("y3_full")
        y3_ready = sem("y3_ready")
        y_stored = sem("y_stored")

        pieces = [VG[g] if v else SG[g] for v, g in GROUPS]

        def prod(j, g):
            return prod0[j % 2][:, :] if g == 0 else prod_rest[:, g - 1, :]

        def count(ck, per_chunk, more):
            return ck[0] * per_chunk + (ck[1] * per_chunk + more)

        block = ctx.enter_context(nc.Block())

        @block.sync
        def _(sp):
            def at_column(ck, more):
                col = count(ck, CHUNK, more)
                return col if isinstance(col, int) else sp.snap(col)

            def window(t, ck):
                return bass.AP(xrows.tensor, at_column(ck, t * SPT * N), [[N, rows_of(t) // F], [N, F], [1, CHUNK]])

            def load_shift(t, src):
                sp.dma_start(xshift[t][0:rows_of(t), :], src) \
                  .then_inc(xshift_loaded[t], 16)

            def load_base(par, ck):
                src = bass.AP(xrows.tensor, at_column(ck, 0), [[0, SPT], [N, F], [1, CHUNK]])
                sp.dma_start(xbase[par][:, :], src).then_inc(xbase_loaded[par], 16)

            def load_cols(par, ck):
                sp.dma_start(xcol[par][:, :], xcols[:, bass.ds(count(ck, TPC * F, 0), TPC * F)]) \
                  .then_inc(xcol_loaded[par], 16)

            def load_diag(par, tile):
                sp.dma_start(xd[par][:, :], xdiag[:, bass.ds(tile, BT * F1)]).then_inc(xd_loaded[par], 16)

            sp.dma_start(w0pair[0], w0[0, :, :]).then_inc(w0_loaded, 16)
            load_base(0, (0, 0))
            for t in range(PT):
                load_shift(t, window(t, (0, 0)))
                if t == 0:
                    sp.dma_start(w0pair[1], w0[1, :, :]).then_inc(w0_loaded, 16)
            load_cols(0, (0, 0))
            for i, (f, n) in enumerate(pieces):
                sp.dma_start(w1raw[:, f * M:(f + n) * M], w1[:, f * M:(f + n) * M]).then_inc(w1_loaded[i], 16)
            load_base(1, (1, 0))
            for t in range(PT):
                sp.wait_ge(zl_ready, t + 1)
                load_shift(t, window(t, (1, 0)))
            load_cols(1, (1, 0))
            load_diag(0, 0)
            load_diag(1, BT * F1)
            sp.dma_start(w2s[:, :], w2[:, :]).then_inc(w2_loaded, 16)

            def chunk(ck, par, first=False, last=False, tail=False):
                if not first and not last:
                    sp.wait_ge(x2_ready, count(ck, TPC, 0))
                    load_cols(1 - par, (ck[0], ck[1] + 1))
                for j in range(TPC):
                    if not last and not tail:
                        if j == 0:
                            load_base(par, (ck[0], ck[1] + 2))
                        for t in range(PT):
                            if ZL_AFTER[t] // NV == j:
                                src = window(t, (ck[0], ck[1] + 2))
                                sp.wait_ge(zl_ready, count(ck, PT, PT + t + 1))
                                load_shift(t, src)
                    if not (first and j == 0) and not (last and j == TPC - 1):
                        sp.wait_ge(S_full, count(ck, TPC, j))
                        load_diag((j + 1) % 2, count(ck, TPC * BT * F1, (j + 1) * BT * F1))

            chunk((0, 0), 0, first=True)
            with sp.Fori(1, CHUNKS - 4, 2) as c:
                chunk((c, 0), 1)
                chunk((c, 1), 0)
            chunk((CHUNKS - 3, 0), 1)
            chunk((CHUNKS - 2, 0), 0, tail=True)
            chunk((CHUNKS - 1, 0), 1, last=True)
            sp.wait_ge(l1_free, CHUNKS)
            sp.dma_start(yt[0:M, :], y1[:, :]).then_inc(y_stored, 16)
            sp.wait_ge(S_stored, CHUNKS * TPC)
            sp.dma_start(yt[M:2 * M, :], S[:, F, :]).then_inc(y_stored, 16)
            sp.wait_ge(y3_ready, 1)
            sp.dma_start(yt[2 * M:3 * M, :], y3).then_inc(y_stored, 16)
            sp.wait_ge(y_stored, 3 * 16)

        @block.tensor
        def _(pe):
            def layer1(t, ck):
                r = rows_of(t)
                wc = slice(t * M, (t + 1) * M)
                pe.wait_ge(zl_ready, count(ck, PT, t + 1))
                h, l = zh[t % ZR][0:r, :], zl[t % ZR][0:r, :]
                pe.matmul(l1bank[:, :], w0h[0:r, wc], h, start=(t == 0), stop=False)
                pe.matmul(l1bank[:, :], w0h[0:r, wc], l, start=False, stop=False)
                pe.matmul(l1bank[:, :], w0l[0:r, wc], h, start=False, stop=(t == PT - 1)).then_inc(l1_steps, 1)

            def scores(ck, par, j, i, first):
                v, g = GROUPS[i]
                if v:
                    per, bank, places, full, done, (f, n) = NV, vbank, V_BANK, v_full, v_done, VG[g]
                else:
                    per, bank, places, full, done, (f, n) = NS, sbank, S_BANK, s_full, s_done, SG[g]
                g2 = per * (j % 2) + g
                back = uses_back(places, g2)
                if not (first and per * j + g < back):
                    pe.wait_ge(done, count(ck, per * TPC, per * j + g - back + 1))
                out = bank[places[g2]][:, 0:n * M]
                cols = slice(j * TILE, (j + 1) * TILE)
                wc = slice(f * M, (f + n) * M)
                if first and j == 0:
                    pe.wait_ge(w1h_ready, i + 1)
                pe.matmul(out, x1h[par][:, cols], w1h[:, wc], start=True, stop=False)
                pe.matmul(out, x1l[par][:, cols], w1h[:, wc], start=False, stop=False)
                if first and j == 0:
                    pe.wait_ge(w1l_ready, i + 1)
                pe.matmul(out, x1h[par][:, cols], w1l[:, wc], start=False, stop=True).then_inc(full, 1)

            def sum_d(ck, j, only=False):
                par = j % 2
                pe.wait_ge(x2_ready, count(ck, TPC, j + 1))
                pe.wait_ge(xd_loaded[par], count(ck, 16 * TPC // 2, 16 * (j // 2 + 1)))
                if not only:
                    pe.wait_ge(S_stored, count(ck, TPC, j))
                pe.matmul(Sbank[:, 0:BT * F1], x2[par][:, :], xd[par][:, :], start=True, stop=True).then_inc(S_full, 1)

            def chunk(ck, par, first=False, last=False):
                pe.wait_ge(x1h_ready, count(ck, 1, 1))
                pe.wait_ge(x1l_ready, count(ck, 1, 1))
                for j in range(TPC):
                    for i, (v, g) in enumerate(GROUPS):
                        scores(ck, par, j, i, first)
                        if i == NG - 1 and not (first and j == 0):
                            sum_d(ck, j - 1, only=first and j == 1)
                        for t in range(PT):
                            if not last and v and L1_AFTER[t] == NV * j + g:
                                if t == 0:
                                    pe.wait_ge(l1_free, count(ck, 1, 1))
                                layer1(t, (ck[0], ck[1] + 1))

            pe.wait_ge(w0h_ready, 1)
            pe.wait_ge(w0l_ready, 1)
            for t in range(PT):
                layer1(t, (0, 0))
            chunk((0, 0), 0, first=True)
            with pe.Fori(1, CHUNKS - 2, 2) as c:
                chunk((c, 0), 1)
                chunk((c, 1), 0)
            chunk((CHUNKS - 1, 0), 1, last=True)
            sum_d((CHUNKS - 1, 0), TPC - 1)
            pe.wait_ge(w2_loaded, 16)
            pe.wait_ge(S_stored, CHUNKS * TPC)
            for f in range(F):
                mm = pe.matmul(l1bank[:, :], w2s[:, f * M:(f + 1) * M], S[:, f, :], start=(f == 0), stop=(f == F - 1))
            mm.then_inc(y3_full, 1)

        @block.scalar
        def _(act):
            def split_x1(ck, par):
                act.wait_ge(l1_steps, count(ck, PT, PT))
                act.activation(x1h[par][:, :], l1bank[:, :], ACT.Copy).then_inc(x1h_ready, 1)

            def store_S(ck, j):
                act.wait_ge(S_full, count(ck, TPC, j + 1))
                act.activation(S[:, :, bass.ds(count(ck, BC, j * BT), BT)],
                               Sbank[:, 0:BT * F1].rearrange("p (b f) -> p f b", f=F1), ACT.Copy).then_inc(S_stored, 1)

            def heads(t, ck, first=False):
                r = rows_of(t)
                act.wait_ge(z_ready, count(ck, PT, t + 1))
                if not (first and t < ZR):
                    act.wait_ge(l1_steps, count(ck, PT, max(t - ZR + 1, 0)))
                act.activation(zh[t % ZR][0:r, :], xshift[t][0:r, :], ACT.Copy).then_inc(zh_ready, 1)

            def chunk(ck, par, first=False, last=False):
                act.wait_ge(xcol_loaded[par], count(ck, 8, 8 if par else 16))
                for j in range(TPC):
                    for g, (f0, n) in enumerate(SG):
                        if g == 0 and not (first and j < 2):
                            act.wait_ge(q_ready, count(ck, TPC, j - 1))
                        if g > 0 and not (first and j < 1):
                            act.wait_ge(pool_step, count(ck, TPC * STEPS, (j - 1) * STEPS + PROD_FREE[g]))
                        act.wait_ge(s_full, count(ck, NS * TPC, NS * j + g + 1))
                        for i in range(n):
                            op = act.activation(prod(j, g)[:, i * M:(i + 1) * M],
                                                sbank[S_BANK[NS * (j % 2) + g]][:, i * M:(i + 1) * M], ACT.Copy,
                                                scale=xcol[par][:, j * F + f0 + i:j * F + f0 + i + 1])
                        op.then_inc(s_done, 1)
                        if g == 1 and not (first and j < 2):
                            store_S(ck, j - 2)
                        for t in range(PT):
                            if not last and ZH_AFTER[t] == NS * j + g:
                                heads(t, (ck[0], ck[1] + 1))
                        if not last and X1H_AFTER == NS * j + g:
                            split_x1((ck[0], ck[1] + 1), 1 - par)

            act.wait_ge(w0sym_ready, 1)
            act.activation(w0h[:, :], w0sym, ACT.Copy).then_inc(w0h_ready, 1)
            for t in range(PT):
                heads(t, (0, 0), first=True)
            for i, (f, n) in enumerate(pieces):
                act.wait_ge(w1_loaded[i], 16)
                act.activation(w1h[:, f * M:(f + n) * M], w1raw[:, f * M:(f + n) * M], ACT.Copy).then_inc(w1h_ready, 1)
            split_x1((0, 0), 0)
            chunk((0, 0), 0, first=True)
            with act.Fori(1, CHUNKS - 2, 2) as c:
                chunk((c, 0), 1)
                chunk((c, 1), 0)
            chunk((CHUNKS - 1, 0), 1, last=True)
            for j in range(TPC - 2, TPC):
                store_S((CHUNKS - 1, 0), j)
            act.wait_ge(y3_full, 1)
            act.activation(y3, l1bank[:, :], ACT.Copy).then_inc(y3_ready, 1)

        @block.vector
        def _(dve):
            def products(t, ck, par):
                r = rows_of(t)
                if t == 0:
                    dve.wait_ge(xbase_loaded[par], count(ck, 8, 8 if par else 16))
                dve.wait_ge(xshift_loaded[t], count(ck, 16, 16))
                dve.tensor_tensor(xshift[t][0:r, :], xbase[par][0:r, :], xshift[t][0:r, :], ALU.mult).then_inc(z_ready, 1)

            def rests(t, ck):
                r = rows_of(t)
                dve.wait_ge(zh_ready, count(ck, PT, t + 1))
                dve.tensor_tensor(zl[t % ZR][0:r, :], xshift[t][0:r, :], zh[t % ZR][0:r, :].bitcast(F32), ALU.subtract) \
                   .then_inc(zl_ready, 1)

            def split_x1(ck, par):
                dve.wait_ge(x1h_ready, count(ck, 1, 1))
                dve.tensor_tensor(x1l[par][:, :], l1bank[:, :], x1h[par][:, :].bitcast(F32), ALU.subtract) \
                   .then_inc(x1l_ready, 1)
                dve.tensor_reduce(y1[:, bass.ds(count(ck, BC, 0), BC)],
                                  l1bank[:, :].rearrange("p (b d) -> p b d", d=D), AX_X, ALU.add).then_inc(l1_free, 1)

            def fold(ck, j):
                H = GF * M // 2
                a = acc[j % 2]
                dve.wait_ge(v_done, count(ck, NV * TPC, NV * (j + 1)))
                dve.tensor_tensor(acc_half[:, :], a[:, 0:H], a[:, H:2 * H], ALU.add).then_inc(half_ready, 1)

            def fold_again(ck, j):
                dve.wait_ge(half_ready, count(ck, TPC, j + 1))
                dve.tensor_tensor(acc_sum[:, :], acc_half[:, 0:M], acc_half[:, M:2 * M], ALU.add).then_inc(sum_ready, 1)

            def finish_x2(ck, j, early=False):
                i = j % 2
                dve.wait_ge(sum_ready, count(ck, TPC, j + 1))
                dve.wait_ge(q_ready, count(ck, TPC, j + 1))
                if not early:
                    dve.wait_ge(S_full, count(ck, TPC, j - 1))
                dve.tensor_tensor(x2[i][:, :], acc_sum[:, :], q[i][:, :], ALU.add).then_inc(x2_ready, 1)

            def scale_and_sum(ck, par, j, g):
                f0, n = VG[g]
                bank = vbank[V_BANK[NV * (j % 2) + g]]
                dve.wait_ge(v_full, count(ck, NV * TPC, NV * j + g + 1))
                for i in range(n):
                    a = acc[j % 2][:, i * M:(i + 1) * M]
                    x = xcol[par][:, j * F + f0 + i:j * F + f0 + i + 1]
                    src = bank[:, i * M:(i + 1) * M]
                    if g == 0:
                        op = dve.tensor_scalar(a, src, x, None, ALU.mult)
                    else:
                        if i == 0:
                            dve.wait_ge(v_half, count(ck, NV * TPC, NV * j + g))
                        if i == n // 2:
                            dve.wait_ge(v_done, count(ck, NV * TPC, NV * j + g))
                        op = dve.scalar_tensor_tensor(a, src, x, a, ALU.mult, ALU.add)
                    if i == n // 2 - 1:
                        op.then_inc(v_half, 1)
                op.then_inc(v_done, 1)

            def chunk(ck, par, first=False, last=False):
                dve.wait_ge(xcol_loaded[par], count(ck, 8, 8 if par else 16))
                for j in range(TPC):
                    for g in range(NV):
                        scale_and_sum(ck, par, j, g)
                        if not (first and j == 0):
                            if g == 0:
                                fold(ck, j - 1)
                            if g == 1:
                                fold_again(ck, j - 1)
                            if g == 2:
                                finish_x2(ck, j - 1, early=first and j < 3)
                        for t in range(PT):
                            if not last and ZL_AFTER[t] == NV * j + g:
                                rests(t, (ck[0], ck[1] + 1))
                            if not last and Z_AFTER[t] == NV * j + g:
                                products(t, (ck[0], ck[1] + 1), 1 - par)
                        if not last and X1L_AFTER == NV * j + g:
                            split_x1((ck[0], ck[1] + 1), 1 - par)

            dve.wait_ge(w0_loaded, 32)
            dve.tensor_tensor(w0sym, w0pair[0], w0pair[1], ALU.add).then_inc(w0sym_ready, 1)
            products(0, (0, 0), 0)
            dve.wait_ge(w0h_ready, 1)
            dve.tensor_tensor(w0l[:, :], w0sym, w0h[:, :].bitcast(F32), ALU.subtract).then_inc(w0l_ready, 1)
            for t in range(PT):
                if t + 1 < PT:
                    products(t + 1, (0, 0), 0)
                rests(t, (0, 0))
            for i, (f, n) in enumerate(pieces):
                if i == NG // 2:
                    split_x1((0, 0), 0)
                wc = slice(f * M, (f + n) * M)
                dve.wait_ge(w1h_ready, i + 1)
                dve.tensor_tensor(w1l[:, wc], w1raw[:, wc], w1h[:, wc].bitcast(F32), ALU.subtract).then_inc(w1l_ready, 1)
            chunk((0, 0), 0, first=True)
            with dve.Fori(1, CHUNKS - 2, 2) as c:
                chunk((c, 0), 1)
                chunk((c, 1), 0)
            chunk((CHUNKS - 1, 0), 1, last=True)
            fold((CHUNKS - 1, 0), TPC - 1)
            fold_again((CHUNKS - 1, 0), TPC - 1)
            finish_x2((CHUNKS - 1, 0), TPC - 1)

        @block.gpsimd
        def _(pool):
            def sum_products(ck, j, early=False):
                n = SG[-1][1] * M
                p = [prod(j, g) for g in range(NS)]
                H = GF * M // 2

                def wait_groups(k):
                    pool.wait_ge(s_done, count(ck, NS * TPC, NS * j + k))

                def add(out, a, b, after=None):
                    if after:
                        pool.wait_ge(pool_step, count(ck, TPC * STEPS, STEPS * j + after))
                    return pool.tensor_tensor(out, a, b, ALU.add)

                wait_groups(2)
                add(p[0], p[0], p[1]).then_inc(pool_step, 1)
                wait_groups(4)
                add(p[2], p[2], p[3]).then_inc(pool_step, 1)
                add(p[0], p[0], p[2], after=2).then_inc(pool_step, 1)
                wait_groups(6)
                add(p[4][:, 0:n], p[4][:, 0:n], p[5][:, 0:n]).then_inc(pool_step, 1)
                add(p[0], p[0], p[4], after=4).then_inc(pool_step, 1)
                add(p[0][:, 0:H], p[0][:, 0:H], p[0][:, H:2 * H], after=5).then_inc(pool_step, 1)
                if not early:
                    pool.wait_ge(x2_ready, count(ck, TPC, j - 1))
                pool.wait_ge(pool_step, count(ck, TPC * STEPS, STEPS * j + 6))
                add(q[j % 2][:, :], p[0][:, 0:M], p[0][:, M:2 * M]).then_inc(q_ready, 1)

            for j in range(TPC):
                sum_products((0, 0), j, early=j < 2)
            with pool.Fori(1, CHUNKS) as c:
                for j in range(TPC):
                    sum_products((c, 0), j)


_INS = ["xrows", "xcols", "xdiag", "w0", "w1", "w2"]


def kernel(r_inputs, L0_rec_f0, L0_rec_f1, L0_rec_f2):
    import numpy as np
    import concourse.bacc as bacc
    from concourse import mybir as mb
    from concourse.bass_utils import run_bass_kernel_spmd

    x = np.asarray(r_inputs)
    f0 = np.asarray(L0_rec_f0).reshape(F, F, M)
    rows = x.transpose(1, 0, 2).reshape(F, N)
    xrows = np.concatenate([rows, rows[:SHIFTS]], axis=0)
    tiles = x.transpose(0, 2, 1).reshape(N // TILE, TILE, F)
    xcols = tiles.transpose(1, 0, 2).reshape(TILE, -1)
    diag = np.zeros((TILE, N // TILE, BT, F1), x.dtype)
    for b in range(BT):
        diag[b * D:(b + 1) * D, :, b, :F] = tiles[:, b * D:(b + 1) * D, :].transpose(1, 0, 2)
        diag[b * D:(b + 1) * D, :, b, F] = 1
    w0 = np.zeros((2, PT * SPT, F, M), f0.dtype)
    fs = np.arange(F)
    for s in range(SHIFTS):
        w0[0, s] = f0[fs, (fs + s) % F]
        if s:
            w0[1, s] = f0[(fs + s) % F, fs]
    w0 = w0.reshape(2, PT, ROWS, M).transpose(0, 2, 1, 3).reshape(2, ROWS, PT * M)
    w1, w2 = (np.asarray(w).reshape(F, M, M).transpose(1, 0, 2).reshape(M, F * M) for w in (L0_rec_f1, L0_rec_f2))

    arrays = {n: np.ascontiguousarray(a) for n, a in zip(_INS, (xrows, xcols, diag.reshape(TILE, -1), w0, w1, w2))}
    nc = bacc.Bacc("TRN2", target_bir_lowering=False, num_devices=1)
    args = [nc.dram_tensor(n, a.shape, mb.dt.from_np(a.dtype), kind="ExternalInput").ap() for n, a in arrays.items()]
    yt = nc.dram_tensor("yt", (3 * M, B), mb.dt.float32, kind="ExternalOutput").ap()
    cin(nc, *args, yt)
    r = run_bass_kernel_spmd(nc, [arrays], core_ids=[0])
    return np.ascontiguousarray(r.results[0]["yt"].T)
```

```python
from contextlib import ExitStack

import concourse.bass as bass
from concourse import mybir

ALU = mybir.AluOpType
ACT = mybir.ActivationFunctionType
F32 = mybir.dt.float32
F32R = mybir.dt.float32r
AX_X = mybir.AxisListType.X

B, F, D, M = 512, 39, 16, 128
N = B * D
P = 128
CHUNK = 512
CHUNKS = N // CHUNK
TILE = 128
TPC = CHUNK // TILE
BT = TILE // D
BC = CHUNK // D
SHIFTS = F // 2 + 1
SPT = P // F
ROWS = SPT * F
PT = -(-SHIFTS // SPT)
F1 = F + 1
GF = 4
FV = 16
VG = [(f, GF) for f in range(0, FV, GF)]
SG = [(f, min(GF, F - f)) for f in range(FV, F, GF)]
NV, NS = len(VG), len(SG)
NG = NV + NS
IS_V = [0, 1, 0, 1, 0, 1, 0, 1, 0, 0]
GROUPS = []
for v in IS_V:
    GROUPS.append((v, sum(1 for k, _ in GROUPS if k == v)))
V_BANK = [0, 1, 2, 0, 1, 2, 0, 1]
S_BANK = [0, 1, 2, 0, 1, 2] * 2
RING = 3
ZR = 2

Z_AFTER = [0, 1, 2, 4, 5, 6, 8]
ZH_AFTER = [1, 3, 4, 7, 9, 10, 13]
ZL_AFTER = [1, 2, 4, 5, 6, 8, 9]
L1_AFTER = [4, 5, 6, 8, 9, 10, 12]
SUM_AFTER = 2
STORE_AFTER = 3
X1_AT = 5
X1H_AFTER = (TPC - 1) * NS + 1
STEPS = 6
PROD_FREE = [None, 1, 3, 2, 5, 4]
X1L_AFTER = (TPC - 1) * NV + 1


def rows_of(t):
    return F * min(SPT, SHIFTS - SPT * t)


def uses_back(places, i):
    return next(k for k in range(1, len(places) + 1) if places[(i - k) % len(places)] == places[i])


def cin(nc, xrows, xcols, xdiag, w0, w1, w2, yt):
    with ExitStack() as ctx:
        def sb(name, shape, dt=F32):
            return ctx.enter_context(nc.sbuf_tensor(name, shape, dt))

        def ps(name):
            return ctx.enter_context(nc.psum_tensor(name, [P, 512], F32))

        def sem(name):
            return ctx.enter_context(nc.semaphore(name))

        w1h = sb("w1h", [P, F * M], F32R)
        w1l = sb("w1l", [P, F * M], F32R)
        w2s = sb("w2s", [P, F * M])
        S = sb("S", [P, F1, B])
        staging = S[:, :, :].rearrange("p f b -> p (f b)")
        w1raw = staging[:, 0:F * M]
        w0pair = [staging[0:ROWS, F * M + i * PT * M:F * M + (i + 1) * PT * M] for i in range(2)]
        w0sym = staging[0:ROWS, F * M + 2 * PT * M:F * M + 3 * PT * M]
        w0h = sb("w0h", [ROWS, PT * M], F32R)
        w0l = sb("w0l", [ROWS, PT * M], F32R)
        xshift = [sb(f"xshift{t}", [ROWS, CHUNK]) for t in range(PT)]
        xbase = [sb(f"xbase{i}", [ROWS, CHUNK]) for i in range(2)]
        zh = [sb(f"zh{i}", [ROWS, CHUNK], F32R) for i in range(ZR)]
        zl = [sb(f"zl{i}", [ROWS, CHUNK], F32R) for i in range(ZR)]
        x1h = [sb(f"x1h{i}", [P, CHUNK], F32R) for i in range(2)]
        x1l = [sb(f"x1l{i}", [P, CHUNK], F32R) for i in range(2)]
        xcol = [sb(f"xcol{i}", [P, TPC * F]) for i in range(2)]
        xd = [sb(f"xd{i}", [P, BT * F1]) for i in range(2)]
        acc = [sb(f"acc{i}", [P, GF * M]) for i in range(2)]
        acc_half = sb("acc_half", [P, GF * M // 2])
        acc_sum = sb("acc_sum", [P, M])
        prod0 = [sb(f"prod0{i}", [P, GF * M]) for i in range(2)]
        prod_rest = sb("prod_rest", [P, NS - 1, GF * M])
        q = [sb(f"q{i}", [P, M]) for i in range(2)]
        x2 = [sb(f"x2{i}", [P, M]) for i in range(2)]
        y1 = sb("y1", [P, B])
        y3 = prod0[0][:, :]

        vbank = [ps(f"vbank{i}") for i in range(RING)]
        sbank = [ps(f"sbank{i}") for i in range(RING)]
        l1bank = ps("l1bank")
        Sbank = ps("Sbank")

        w0_loaded = sem("w0_loaded")
        w1_loaded = [sem(f"w1_loaded{i}") for i in range(NG)]
        w2_loaded = sem("w2_loaded")
        xshift_loaded = [sem(f"xshift_loaded{t}") for t in range(PT)]
        xbase_loaded = [sem(f"xbase_loaded{i}") for i in range(2)]
        xcol_loaded = [sem(f"xcol_loaded{i}") for i in range(2)]
        xd_loaded = [sem(f"xd_loaded{i}") for i in range(2)]
        w0sym_ready = sem("w0sym_ready")
        w0h_ready = sem("w0h_ready")
        w0l_ready = sem("w0l_ready")
        w1h_ready = sem("w1h_ready")
        w1l_ready = sem("w1l_ready")
        z_ready = sem("z_ready")
        zh_ready = sem("zh_ready")
        zl_ready = sem("zl_ready")
        l1_steps = sem("l1_steps")
        x1h_ready = sem("x1h_ready")
        x1l_ready = sem("x1l_ready")
        l1_free = sem("l1_free")
        v_full = sem("v_full")
        v_half = sem("v_half")
        v_done = sem("v_done")
        half_ready = sem("half_ready")
        sum_ready = sem("sum_ready")
        s_full = sem("s_full")
        s_done = sem("s_done")
        pool_step = sem("pool_step")
        q_ready = sem("q_ready")
        x2_ready = sem("x2_ready")
        S_full = sem("S_full")
        S_stored = sem("S_stored")
        y3_full = sem("y3_full")
        y3_ready = sem("y3_ready")
        y_stored = sem("y_stored")

        pieces = [VG[g] if v else SG[g] for v, g in GROUPS]

        def prod(j, g):
            return prod0[j % 2][:, :] if g == 0 else prod_rest[:, g - 1, :]

        def count(ck, per_chunk, more):
            return ck[0] * per_chunk + (ck[1] * per_chunk + more)

        def window(t, at):
            return bass.AP(xrows.tensor, at, [[N, rows_of(t) // F], [N, F], [1, CHUNK]])

        def prefetched_loop(engine, start, end, step):
            return nc.Fori(start, end, step, engines=bass.OrderedEngineSet([engine.engine]), hint_back_edge=True)

        block = ctx.enter_context(nc.Block())

        @block.sync
        def _(sp):
            def at_column(ck, more):
                col = count(ck, CHUNK, more)
                return col if isinstance(col, int) else sp.snap(col)

            def load_shift(t, at):
                sp.dma_start(xshift[t][0:rows_of(t), :], window(t, at)).then_inc(xshift_loaded[t], 16)

            def load_base(par, ck):
                src = bass.AP(xrows.tensor, at_column(ck, 0), [[0, SPT], [N, F], [1, CHUNK]])
                sp.dma_start(xbase[par][:, :], src).then_inc(xbase_loaded[par], 16)

            def load_cols(par, ck):
                sp.dma_start(xcol[par][:, :], xcols[:, bass.ds(count(ck, TPC * F, 0), TPC * F)]) \
                  .then_inc(xcol_loaded[par], 16)

            def load_diag(par, tile):
                sp.dma_start(xd[par][:, :], xdiag[:, bass.ds(tile, BT * F1)]).then_inc(xd_loaded[par], 16)

            sp.dma_start(w0pair[0], w0[0, :, :]).then_inc(w0_loaded, 16)
            load_base(0, (0, 0))
            for t in range(0, PT, 2):
                load_shift(t, t * SPT * N)
            for i, (f, n) in enumerate(pieces):
                if i == NG // 2:
                    load_cols(0, (0, 0))
                if i % 2 == 0:
                    sp.dma_start(w1raw[:, f * M:(f + n) * M], w1[:, f * M:(f + n) * M]).then_inc(w1_loaded[i], 16)
            load_base(1, (1, 0))
            for t in range(PT):
                sp.wait_ge(l1_steps, t + 1)
                load_shift(t, t * SPT * N + CHUNK)
            load_cols(1, (1, 0))
            load_diag(0, 0)
            load_diag(1, BT * F1)
            sp.dma_start(w2s[:, :], w2[:, :]).then_inc(w2_loaded, 16)

            def chunk(ck, par, first=False, last=False, tail=False):
                if not first and not last:
                    sp.wait_ge(x2_ready, count(ck, TPC, 0))
                    load_cols(1 - par, (ck[0], ck[1] + 1))
                for j in range(TPC):
                    if not last and not tail:
                        if j == 0:
                            load_base(par, (ck[0], ck[1] + 2))
                        for t in range(PT):
                            if ZL_AFTER[t] // NV == j:
                                at = at_column((ck[0], ck[1] + 2), t * SPT * N)
                                sp.wait_ge(zl_ready, count(ck, PT, t + 1))
                                load_shift(t, at)
                    if not (first and j < 2):
                        sp.wait_ge(S_full, count(ck, TPC, j - 1))
                        load_diag(j % 2, count(ck, TPC * BT * F1, j * BT * F1))

            chunk((0, 0), 0, first=True)
            with sp.Fori(1, CHUNKS - 4, 2) as c:
                chunk((c, 0), 1)
                chunk((c, 1), 0)
            chunk((CHUNKS - 3, 0), 1)
            chunk((CHUNKS - 2, 0), 0, tail=True)
            chunk((CHUNKS - 1, 0), 1, last=True)
            sp.wait_ge(l1_free, CHUNKS)
            sp.dma_start(yt[0:M, :], y1[:, :]).then_inc(y_stored, 16)
            sp.wait_ge(S_stored, CHUNKS * TPC)
            sp.dma_start(yt[M:2 * M, :], S[:, F, :]).then_inc(y_stored, 16)
            sp.wait_ge(y3_ready, 1)
            sp.dma_start(yt[2 * M:3 * M, :], y3).then_inc(y_stored, 16)
            sp.wait_ge(y_stored, 3 * 16)

        @block.tensor
        def _(pe):
            def layer1_plain(t):
                r = rows_of(t)
                pe.wait_ge(z_ready, t + 1)
                pe.matmul(l1bank[:, :], w0sym[0:r, t * M:(t + 1) * M], xshift[t][0:r, :],
                          start=(t == 0), stop=(t == PT - 1)).then_inc(l1_steps, 1)

            def layer1(t, ck):
                r = rows_of(t)
                wc = slice(t * M, (t + 1) * M)
                pe.wait_ge(zl_ready, count(ck, PT, t + 1 - PT))
                h, l = zh[t % ZR][0:r, :], zl[t % ZR][0:r, :]
                pe.matmul(l1bank[:, :], w0h[0:r, wc], h, start=(t == 0), stop=False)
                pe.matmul(l1bank[:, :], w0h[0:r, wc], l, start=False, stop=False)
                pe.matmul(l1bank[:, :], w0l[0:r, wc], h, start=False, stop=(t == PT - 1)).then_inc(l1_steps, 1)

            def scores(ck, par, j, i, first):
                v, g = GROUPS[i]
                if v:
                    per, bank, places, full, done, (f, n) = NV, vbank, V_BANK, v_full, v_done, VG[g]
                else:
                    per, bank, places, full, done, (f, n) = NS, sbank, S_BANK, s_full, s_done, SG[g]
                g2 = per * (j % 2) + g
                back = uses_back(places, g2)
                if not (first and per * j + g < back):
                    pe.wait_ge(done, count(ck, per * TPC, per * j + g - back + 1))
                out = bank[places[g2]][:, 0:n * M]
                cols = slice(j * TILE, (j + 1) * TILE)
                wc = slice(f * M, (f + n) * M)
                if first and j == 0:
                    pe.wait_ge(w1l_ready, i + 1)
                if i % 2 == 0:
                    pe.matmul(out, x1h[par][:, cols], w1h[:, wc], start=True, stop=False)
                    pe.matmul(out, x1h[par][:, cols], w1l[:, wc], start=False, stop=False)
                    if j == 0 and i == 0:
                        pe.wait_ge(x1l_ready, count(ck, 1, 1))
                    pe.matmul(out, x1l[par][:, cols], w1h[:, wc], start=False, stop=True).then_inc(full, 1)
                else:
                    pe.matmul(out, x1l[par][:, cols], w1h[:, wc], start=True, stop=False)
                    pe.matmul(out, x1h[par][:, cols], w1h[:, wc], start=False, stop=False)
                    pe.matmul(out, x1h[par][:, cols], w1l[:, wc], start=False, stop=True).then_inc(full, 1)

            def sum_d(ck, j, only=False):
                par = j % 2
                pe.wait_ge(x2_ready, count(ck, TPC, j + 1))
                pe.wait_ge(xd_loaded[par], count(ck, 16 * TPC // 2, 16 * (j // 2 + 1)))
                if not only:
                    pe.wait_ge(S_stored, count(ck, TPC, j))
                pe.matmul(Sbank[:, 0:BT * F1], x2[par][:, :], xd[par][:, :], start=True, stop=True).then_inc(S_full, 1)

            def layer3(b0, b1, between=None):
                for f in range(F):
                    if between and f in between:
                        sum_d((CHUNKS - 1, 0), between[f])
                    mm = pe.matmul(l1bank[:, b0:b1], w2s[:, f * M:(f + 1) * M], S[:, f, b0:b1],
                                   start=(f == 0), stop=(f == F - 1))
                mm.then_inc(y3_full, 1)

            def chunk(ck, par, first=False, last=False):
                pe.wait_ge(x1h_ready, count(ck, 1, 1))
                for j in range(TPC):
                    for i, (v, g) in enumerate(GROUPS):
                        scores(ck, par, j, i, first)
                        if i == SUM_AFTER and not (first and j < 2):
                            sum_d(ck, j - 2, only=first and j == 2)
                        for t in range(PT):
                            if not last and v and L1_AFTER[t] == NV * j + g:
                                if t == 0 and first:
                                    pe.wait_ge(w0l_ready, 1)
                                if t == 0:
                                    pe.wait_ge(l1_free, count(ck, 1, 1))
                                layer1(t, (ck[0], ck[1] + 1))

            pe.wait_ge(w0sym_ready, 1)
            for t in range(PT):
                layer1_plain(t)
            chunk((0, 0), 0, first=True)
            with pe.Fori(1, CHUNKS - 2, 2) as c:
                chunk((c, 0), 1)
                chunk((c, 1), 0)
            chunk((CHUNKS - 1, 0), 1, last=True)
            pe.wait_ge(w2_loaded, 16)
            pe.wait_ge(S_stored, CHUNKS * TPC // 2)
            layer3(0, B // 2, between={F // 2: TPC - 2, F - F // 4: TPC - 1})
            pe.wait_ge(S_stored, CHUNKS * TPC)
            layer3(B // 2, B)

        @block.scalar
        def _(act):
            def split_x1(ck, par):
                act.wait_ge(l1_steps, count(ck, PT, PT))
                act.activation(x1h[par][:, :], l1bank[:, :], ACT.Copy).then_inc(x1h_ready, 1)

            def store_S(ck, j):
                act.wait_ge(S_full, count(ck, TPC, j + 1))
                act.activation(S[:, :, bass.ds(count(ck, BC, j * BT), BT)],
                               Sbank[:, 0:BT * F1].rearrange("p (b f) -> p f b", f=F1), ACT.Copy).then_inc(S_stored, 1)

            def heads(t, ck):
                r = rows_of(t)
                act.wait_ge(z_ready, count(ck, PT, t + 1))
                act.wait_ge(l1_steps, count(ck, PT, max(t - ZR + 1, 0)))
                act.activation(zh[t % ZR][0:r, :], xshift[t][0:r, :], ACT.Copy).then_inc(zh_ready, 1)

            def chunk(ck, par, first=False, last=False):
                act.wait_ge(xcol_loaded[par], count(ck, 8, 8 if par else 16))
                for j in range(TPC):
                    for g, (f0, n) in enumerate(SG):
                        if g == 0 and not (first and j < 2):
                            act.wait_ge(q_ready, count(ck, TPC, j - 1))
                        if g > 0 and not (first and j < 1):
                            act.wait_ge(pool_step, count(ck, TPC * STEPS, (j - 1) * STEPS + PROD_FREE[g]))
                        act.wait_ge(s_full, count(ck, NS * TPC, NS * j + g + 1))
                        for i in range(n):
                            op = act.activation(prod(j, g)[:, i * M:(i + 1) * M],
                                                sbank[S_BANK[NS * (j % 2) + g]][:, i * M:(i + 1) * M], ACT.Copy,
                                                scale=xcol[par][:, j * F + f0 + i:j * F + f0 + i + 1])
                        op.then_inc(s_done, 1)
                        if g == STORE_AFTER and not (first and j < 2):
                            store_S(ck, j - 2)
                        for t in range(PT):
                            if not last and ZH_AFTER[t] == NS * j + g:
                                heads(t, (ck[0], ck[1] + 1))
                        if not last and X1H_AFTER == NS * j + g:
                            split_x1((ck[0], ck[1] + 1), 1 - par)

            act.dma_start(w0pair[1], w0[1, :, :]).then_inc(w0_loaded, 16)
            for t in range(1, PT, 2):
                act.dma_start(xshift[t][0:rows_of(t), :], window(t, t * SPT * N)).then_inc(xshift_loaded[t], 16)
            for i, (f, n) in enumerate(pieces):
                if i % 2 == 1:
                    act.dma_start(w1raw[:, f * M:(f + n) * M], w1[:, f * M:(f + n) * M]).then_inc(w1_loaded[i], 16)
            for i, (f, n) in enumerate(pieces):
                act.wait_ge(w1_loaded[i], 16)
                act.activation(w1h[:, f * M:(f + n) * M], w1raw[:, f * M:(f + n) * M], ACT.Copy).then_inc(w1h_ready, 1)
                if i == X1_AT:
                    split_x1((0, 0), 0)
            act.wait_ge(w0sym_ready, 1)
            act.activation(w0h[:, :], w0sym, ACT.Copy).then_inc(w0h_ready, 1)
            chunk((0, 0), 0, first=True)
            with prefetched_loop(act, 1, CHUNKS - 2, 2) as c:
                chunk((c, 0), 1)
                chunk((c, 1), 0)
            chunk((CHUNKS - 1, 0), 1, last=True)
            for j in range(TPC - 2, TPC):
                store_S((CHUNKS - 1, 0), j)
            act.wait_ge(y3_full, 2)
            act.activation(y3, l1bank[:, :], ACT.Copy).then_inc(y3_ready, 1)

        @block.vector
        def _(dve):
            def products(t, ck, par):
                r = rows_of(t)
                if t == 0:
                    dve.wait_ge(xbase_loaded[par], count(ck, 8, 8 if par else 16))
                dve.wait_ge(xshift_loaded[t], count(ck, 16, 16))
                dve.tensor_tensor(xshift[t][0:r, :], xbase[par][0:r, :], xshift[t][0:r, :], ALU.mult).then_inc(z_ready, 1)

            def rests(t, ck):
                r = rows_of(t)
                dve.wait_ge(zh_ready, count(ck, PT, t + 1 - PT))
                dve.tensor_tensor(zl[t % ZR][0:r, :], xshift[t][0:r, :], zh[t % ZR][0:r, :].bitcast(F32), ALU.subtract) \
                   .then_inc(zl_ready, 1)

            def split_x1(ck, par):
                dve.wait_ge(x1h_ready, count(ck, 1, 1))
                dve.tensor_tensor(x1l[par][:, :], l1bank[:, :], x1h[par][:, :].bitcast(F32), ALU.subtract) \
                   .then_inc(x1l_ready, 1)
                dve.tensor_reduce(y1[:, bass.ds(count(ck, BC, 0), BC)],
                                  l1bank[:, :].rearrange("p (b d) -> p b d", d=D), AX_X, ALU.add).then_inc(l1_free, 1)

            def fold(ck, j):
                H = GF * M // 2
                a = acc[j % 2]
                dve.wait_ge(v_done, count(ck, NV * TPC, NV * (j + 1)))
                dve.tensor_tensor(acc_half[:, :], a[:, 0:H], a[:, H:2 * H], ALU.add).then_inc(half_ready, 1)

            def fold_again(ck, j):
                dve.wait_ge(half_ready, count(ck, TPC, j + 1))
                dve.tensor_tensor(acc_sum[:, :], acc_half[:, 0:M], acc_half[:, M:2 * M], ALU.add).then_inc(sum_ready, 1)

            def finish_x2(ck, j, new_buffer=False):
                i = j % 2
                dve.wait_ge(sum_ready, count(ck, TPC, j + 1))
                dve.wait_ge(q_ready, count(ck, TPC, j + 1))
                if not new_buffer:
                    dve.wait_ge(S_full, count(ck, TPC, j - 1))
                dve.tensor_tensor(x2[i][:, :], acc_sum[:, :], q[i][:, :], ALU.add).then_inc(x2_ready, 1)

            def scale_and_sum(ck, par, j, g):
                f0, n = VG[g]
                bank = vbank[V_BANK[NV * (j % 2) + g]]
                dve.wait_ge(v_full, count(ck, NV * TPC, NV * j + g + 1))
                for i in range(n):
                    a = acc[j % 2][:, i * M:(i + 1) * M]
                    x = xcol[par][:, j * F + f0 + i:j * F + f0 + i + 1]
                    src = bank[:, i * M:(i + 1) * M]
                    if g == 0:
                        op = dve.tensor_scalar(a, src, x, None, ALU.mult)
                    else:
                        if i == 0:
                            dve.wait_ge(v_half, count(ck, NV * TPC, NV * j + g))
                        if i == n // 2:
                            dve.wait_ge(v_done, count(ck, NV * TPC, NV * j + g))
                        op = dve.scalar_tensor_tensor(a, src, x, a, ALU.mult, ALU.add)
                    if i == n // 2 - 1:
                        op.then_inc(v_half, 1)
                op.then_inc(v_done, 1)

            def chunk(ck, par, first=False, last=False):
                dve.wait_ge(xcol_loaded[par], count(ck, 8, 8 if par else 16))
                for j in range(TPC):
                    for g in range(NV):
                        scale_and_sum(ck, par, j, g)
                        if not (first and j == 0):
                            if g == 0:
                                fold(ck, j - 1)
                            if g == 1:
                                fold_again(ck, j - 1)
                            if g == 2:
                                finish_x2(ck, j - 1, new_buffer=first and j < 3)
                        for t in range(PT):
                            if not last and ZL_AFTER[t] == NV * j + g:
                                rests(t, (ck[0], ck[1] + 1))
                            if not last and Z_AFTER[t] == NV * j + g:
                                products(t, (ck[0], ck[1] + 1), 1 - par)
                        if not last and X1L_AFTER == NV * j + g:
                            split_x1((ck[0], ck[1] + 1), 1 - par)

            dve.wait_ge(w0_loaded, 32)
            dve.tensor_tensor(w0sym, w0pair[0], w0pair[1], ALU.add).then_inc(w0sym_ready, 1)
            for t in range(PT):
                products(t, (0, 0), 0)
            for i, (f, n) in enumerate(pieces):
                wc = slice(f * M, (f + n) * M)
                dve.wait_ge(w1h_ready, i + 1)
                dve.tensor_tensor(w1l[:, wc], w1raw[:, wc], w1h[:, wc].bitcast(F32), ALU.subtract).then_inc(w1l_ready, 1)
                if i == X1_AT:
                    split_x1((0, 0), 0)
            dve.wait_ge(w0h_ready, 1)
            dve.tensor_tensor(w0l[:, :], w0sym, w0h[:, :].bitcast(F32), ALU.subtract).then_inc(w0l_ready, 1)
            chunk((0, 0), 0, first=True)
            with prefetched_loop(dve, 1, CHUNKS - 2, 2) as c:
                chunk((c, 0), 1)
                chunk((c, 1), 0)
            chunk((CHUNKS - 1, 0), 1, last=True)
            fold((CHUNKS - 1, 0), TPC - 1)
            fold_again((CHUNKS - 1, 0), TPC - 1)
            finish_x2((CHUNKS - 1, 0), TPC - 1)

        @block.gpsimd
        def _(pool):
            def sum_products(ck, j, new_buffer=False):
                n = SG[-1][1] * M
                p = [prod(j, g) for g in range(NS)]
                H = GF * M // 2

                def wait_groups(k):
                    pool.wait_ge(s_done, count(ck, NS * TPC, NS * j + k))

                def add(out, a, b, after=None):
                    if after:
                        pool.wait_ge(pool_step, count(ck, TPC * STEPS, STEPS * j + after))
                    return pool.tensor_tensor(out, a, b, ALU.add)

                wait_groups(2)
                add(p[0], p[0], p[1]).then_inc(pool_step, 1)
                wait_groups(4)
                add(p[2], p[2], p[3]).then_inc(pool_step, 1)
                add(p[0], p[0], p[2], after=2).then_inc(pool_step, 1)
                wait_groups(6)
                add(p[4][:, 0:n], p[4][:, 0:n], p[5][:, 0:n]).then_inc(pool_step, 1)
                add(p[0], p[0], p[4], after=4).then_inc(pool_step, 1)
                add(p[0][:, 0:H], p[0][:, 0:H], p[0][:, H:2 * H], after=5).then_inc(pool_step, 1)
                if not new_buffer:
                    pool.wait_ge(x2_ready, count(ck, TPC, j - 1))
                pool.wait_ge(pool_step, count(ck, TPC * STEPS, STEPS * j + 6))
                add(q[j % 2][:, :], p[0][:, 0:M], p[0][:, M:2 * M]).then_inc(q_ready, 1)

            for j in range(TPC):
                sum_products((0, 0), j, new_buffer=j < 2)
            with prefetched_loop(pool, 1, CHUNKS, 1) as c:
                for j in range(TPC):
                    sum_products((c, 0), j)


_INS = ["xrows", "xcols", "xdiag", "w0", "w1", "w2"]


def kernel(r_inputs, L0_rec_f0, L0_rec_f1, L0_rec_f2):
    import numpy as np
    import concourse.bacc as bacc
    from concourse import mybir as mb
    from concourse.bass_utils import run_bass_kernel_spmd

    x = np.asarray(r_inputs)
    f0 = np.asarray(L0_rec_f0).reshape(F, F, M)
    rows = x.transpose(1, 0, 2).reshape(F, N)
    xrows = np.concatenate([rows, rows[:SHIFTS]], axis=0)
    tiles = x.transpose(0, 2, 1).reshape(N // TILE, TILE, F)
    xcols = tiles.transpose(1, 0, 2).reshape(TILE, -1)
    diag = np.zeros((TILE, N // TILE, BT, F1), x.dtype)
    for b in range(BT):
        diag[b * D:(b + 1) * D, :, b, :F] = tiles[:, b * D:(b + 1) * D, :].transpose(1, 0, 2)
        diag[b * D:(b + 1) * D, :, b, F] = 1
    w0 = np.zeros((2, PT * SPT, F, M), f0.dtype)
    fs = np.arange(F)
    for s in range(SHIFTS):
        w0[0, s] = f0[fs, (fs + s) % F]
        if s:
            w0[1, s] = f0[(fs + s) % F, fs]
    w0 = w0.reshape(2, PT, ROWS, M).transpose(0, 2, 1, 3).reshape(2, ROWS, PT * M)
    w1, w2 = (np.asarray(w).reshape(F, M, M).transpose(1, 0, 2).reshape(M, F * M) for w in (L0_rec_f1, L0_rec_f2))

    arrays = {n: np.ascontiguousarray(a) for n, a in zip(_INS, (xrows, xcols, diag.reshape(TILE, -1), w0, w1, w2))}
    nc = bacc.Bacc("TRN2", target_bir_lowering=False, num_devices=1)
    args = [nc.dram_tensor(n, a.shape, mb.dt.from_np(a.dtype), kind="ExternalInput").ap() for n, a in arrays.items()]
    yt = nc.dram_tensor("yt", (3 * M, B), mb.dt.float32, kind="ExternalOutput").ap()
    cin(nc, *args, yt)
    r = run_bass_kernel_spmd(nc, [arrays], core_ids=[0])
    return np.ascontiguousarray(r.results[0]["yt"].T)
```
